# Optimizing a Trainium2 kernel written in Bass

```python
import numpy as np
import jax
import jax.numpy as jnp

def _softmax(x, axis=-1):
    return jax.nn.softmax(x, axis=axis)

def _gelu(x):
    return jax.nn.gelu(x, approximate=True)

def _silu(x):
    return jax.nn.silu(x)

def _sigmoid(x):
    return jax.nn.sigmoid(x)

def _layernorm(x, axis=-1, eps=1e-05):
    m = jnp.mean(x, axis=axis, keepdims=True)
    v = jnp.var(x, axis=axis, keepdims=True)
    return (x - m) / jnp.sqrt(v + eps)

def _scatter_add(tgt, idx, src, axis=0):
    return tgt.at[idx].add(src)

def _segment_sum(src, seg, n):
    return jax.ops.segment_sum(src, seg, n)
kernel_name = 'mk_adj_preln_d1_adj_r2_890202'

def setup_inputs(seed: int=0):
    np.random.seed(seed)
    _w = jnp.asarray

    def _rec_inputs():
        import jax
        import jax.numpy as jnp
        _gk = jax.random.key(seed)
        x = -0.0005207 + 1.001 * jax.random.normal(jax.random.fold_in(_gk, 1), (8192, 128), jnp.float32)
        _a = jax.random.bernoulli(jax.random.fold_in(_gk, 2), 0.000976562, (8192, 8192))
        _a = jnp.logical_or(_a, jnp.swapaxes(_a, -1, -2))
        _a = jnp.logical_or(_a, jnp.eye(8192, dtype=bool))
        _af = _a.astype(jnp.float32)
        _af = _af * jax.random.uniform(jax.random.fold_in(_gk, 3), (8192, 8192), jnp.float32, 0.05, 1)
        adj = _af
        return (x, adj)
    x, adj = _rec_inputs()

    def _L0_gnn_setup():
        import jax, jax.numpy as jnp
        import numpy as np
        N = 8192
        IN_DIM = 128
        OUT_DIM = 128

        def _message(X, A, W):
            deg = jnp.sum(A, axis=1, keepdims=True)
            A_norm = A / jnp.where(deg > 0, deg, 1.0)
            return A_norm @ X @ W
        key = jax.random.key(seed)
        k1, k2, k3, k4 = jax.random.split(key, 4)
        X = jax.random.normal(k1, (N, IN_DIM), dtype=jnp.float32)
        A = jax.random.uniform(k2, (N, N), dtype=jnp.float32)
        W_in = jax.random.normal(k3, (IN_DIM, OUT_DIM), dtype=jnp.float32) / np.sqrt(IN_DIM)
        W_out = jax.random.normal(k4, (IN_DIM, OUT_DIM), dtype=jnp.float32) / np.sqrt(IN_DIM)
        return {'X': X, 'A': A, 'W_in': W_in, 'W_out': W_out}
    _L0_gnn_all = _L0_gnn_setup()
    _L0_gnn_in = {k: v for k, v in _L0_gnn_all.items() if k in ('W_in', 'W_out')}
    del _L0_gnn_all
    return {'x': x, 'adj': adj, 'L0_gnn_W_in': _L0_gnn_in['W_in'], 'L0_gnn_W_out': _L0_gnn_in['W_out']}

def reference(x, adj, L0_gnn_W_in, L0_gnn_W_out):
    import jax
    import jax.numpy as jnp

    def _L0_gnn_ref(X, A, W_in, W_out):
        import jax, jax.numpy as jnp
        import numpy as np
        N = 8192
        IN_DIM = 128
        OUT_DIM = 128

        def _message(X, A, W):
            deg = jnp.sum(A, axis=1, keepdims=True)
            A_norm = A / jnp.where(deg > 0, deg, 1.0)
            return A_norm @ X @ W
        X_in = _message(X, A, W_in)
        X_out = _message(X, A.T, W_out)
        return X_in + X_out
    h = jnp.maximum(_layernorm(x, axis=-1), 0.0)
    x = x + _L0_gnn_ref(h, adj, L0_gnn_W_in, L0_gnn_W_out)
    return x

_drawn_inputs = setup_inputs


def setup_inputs(seed=0):
    import zlib

    import numpy as np

    out = dict(_drawn_inputs(seed))
    spreads = {}
    factors = {}
    for name, (base, spread) in spreads.items():
        noise = np.random.default_rng([zlib.crc32(name.encode()), seed]).standard_normal(out[name].shape)
        drawn = base * np.exp(spread * noise) if base else spread * noise
        out[name] = jnp.asarray(drawn.astype(out[name].dtype))
    for name, factor in factors.items():
        out[name] = (out[name] * factor).astype(out[name].dtype)
    return out
```

```python
from contextlib import ExitStack

import concourse.bass as bass
from concourse import mybir

P = 128
LN_EPS = 1e-5


def gnn_layer_kernel(nc: bass.Bass, x: bass.AP, adj: bass.AP, w_in: bass.AP, w_out: bass.AP, out: bass.AP):
    F32 = mybir.dt.float32
    F32R = mybir.dt.float32r
    ALU = mybir.AluOpType
    ACT = mybir.ActivationFunctionType
    AX = mybir.AxisListType

    N, D = x.shape
    Q = 4
    BW = Q * P
    PANELS = N // BW
    BLOCKS = N // BW
    TILES = N // P
    UP = Q * BLOCKS
    RAW = 4
    RING = 4
    AHEAD = 2
    assert D == P and PANELS == BLOCKS and BLOCKS % RAW == 0 and UP % RING == 0

    x_tiles = x.rearrange("(t p) d -> p t d", p=P)
    out_tiles = out.rearrange("(t p) d -> p t d", p=P)
    adj_panels = adj.rearrange("(n q p) c -> n p q c", q=Q, p=P)

    ctx = ExitStack()
    with ctx:
        def sb(name, shape, dt=F32):
            return ctx.enter_context(nc.sbuf_tensor(name, shape, dt))

        def pb(name):
            return ctx.enter_context(nc.psum_tensor(name, [P, BW], F32))

        def sem(name):
            return ctx.enter_context(nc.semaphore(name))

        xy = sb("xy", [P, TILES, D])
        h_hi = sb("h_hi", [P, TILES, D], F32R)
        h_lo = sb("h_lo", [P, TILES, D], F32R)
        acc2 = sb("acc2", [P, N])
        w_in_sb = sb("w_in_sb", [P, D])
        w_out_sb = sb("w_out_sb", [P, D])
        ident = sb("ident", [P, P])
        colsum = sb("colsum", [P, TILES, PANELS])
        rowsum = sb("rowsum", [P, Q, BLOCKS])

        raw = sb("raw", [P, RAW, Q, BW])
        row_hi = sb("row_hi", [P, RING, BW], F32R)
        row_lo = sb("row_lo", [P, RING, BW], F32R)
        col_hi = sb("col_hi", [P, RING, BW], F32R)
        col_lo = sb("col_lo", [P, RING, BW], F32R)
        hp_hi = sb("hp_hi", [P, Q, D], F32R)
        hp_lo = sb("hp_lo", [P, Q, D], F32R)
        out1_sb = sb("out1_sb", [P, BW])
        stats = sb("stats", [P, Q, 6])
        mean_var = sb("mean_var", [P, TILES, 2])
        var_eps = sb("var_eps", [P, TILES])
        std = sb("std", [P, TILES])
        rstd = sb("rstd", [P, TILES])
        tmp = sb("tmp", [P, Q])
        tmp2 = sb("tmp2", [P, Q])
        row_deg = sb("row_deg", [P, Q])
        col_deg = sb("col_deg", [P, Q])
        rdeg = sb("rdeg", [P, Q])

        tr = [pb(f"tr{i}") for i in range(RING)]
        out2 = [pb("out2a"), pb("out2b")]
        out1 = pb("out1")
        proj = pb("proj")

        x_loaded = [sem(f"x_loaded{c}") for c in range(BLOCKS)]
        w_loaded = sem("w_loaded")
        raw_loaded = [sem(f"raw_loaded{r}") for r in range(RAW)]
        ident_zeroed = sem("ident_zeroed")
        ident_ready = sem("ident_ready")
        acc2_zeroed = sem("acc2_zeroed")
        chunk_var = sem("chunk_var")
        chunk_std = sem("chunk_std")
        chunk_norm = sem("chunk_norm")
        chunk_hi = sem("chunk_hi")
        chunk_h = sem("chunk_h")
        hp_copied = sem("hp_copied")
        transposed = sem("transposed")
        row_hi_done = sem("row_hi_done")
        row_lo_done = sem("row_lo_done")
        col_hi_done = sem("col_hi_done")
        col_lo_done = sem("col_lo_done")
        row_used = sem("row_used")
        col_used = sem("col_used")
        acc2_added = sem("acc2_added")
        out1_copied = sem("out1_copied")
        proj_ready = sem("proj_ready")
        proj_used = sem("proj_used")
        rowsum_read = sem("rowsum_read")
        h_step, norm_step, row_step, col_step = sem("h_step"), sem("norm_step"), sem("row_step"), sem("col_step")
        out_stored = sem("out_stored")

        norm = out1_sb[:, :].rearrange("p (q d) -> p q d", q=Q)

        block = ctx.enter_context(nc.Block())

        def wait(eng, semaphore, value):
            if not isinstance(value, int) or value > 0:
                eng.wait_ge(semaphore, value)

        LAST = PANELS - 1
        H_STEPS = 2 * Q
        N_STEPS = 5

        @block.sync
        def _(sp):
            def load_x(c):
                sp.dma_start(xy[:, Q * c:Q * c + Q, :], x_tiles[:, Q * c:Q * c + Q, :]).then_inc(x_loaded[c], 16)

            def load_blocks(p):
                for b in range(BLOCKS):
                    wait(sp, transposed, UP * p + Q * (b - RAW + 1))
                    wait(sp, row_lo_done, UP * p + Q * (b - RAW + 1))
                    if isinstance(p, int) and p == 0 and b + 2 < BLOCKS:
                        load_x(b + 2)
                    src = adj_panels[p] if isinstance(p, int) else adj_panels[bass.ds(p, 1)].rearrange("a p q c -> (a p) q c")
                    sp.dma_start(raw[:, b % RAW], src[:, :, BW * b:BW * b + BW]).then_inc(raw_loaded[b % RAW], 16)

            load_x(0)
            load_x(1)
            load_blocks(0)
            with sp.Fori(1, PANELS) as p:
                load_blocks(p)
            for c in range(BLOCKS):
                sp.wait_ge(proj_used, LAST + c + 1 if c < BLOCKS - 1 else PANELS + BLOCKS)
                sp.dma_start(out_tiles[:, Q * c:Q * c + Q, :], xy[:, Q * c:Q * c + Q, :]).then_inc(out_stored, 16)
            sp.wait_ge(out_stored, 16 * BLOCKS)

        @block.gpsimd
        def _(pool):
            nc.gpsimd.memset(ident[:, :], 0.0).then_inc(ident_zeroed, 1)
            pool.wait_ge(ident_zeroed, 1)
            nc.gpsimd.affine_select(out=ident[:, :], in_=ident[:, :], compare_op=ALU.not_equal, fill=1.0, base=0,
                                    pattern=[[-1, P]], channel_multiplier=1).then_inc(ident_ready, 1)
            nc.gpsimd.memset(acc2[:, :], 0.0).then_inc(acc2_zeroed, 1)

            def copy_panel_h(p):
                for q in range(Q):
                    wait(pool, row_used, UP * (p - 1) + UP - Q + q + 1)
                    pool.wait_ge(chunk_h, p + 1)
                    nc.gpsimd.tensor_copy(hp_hi[:, q:q + 1, :], h_hi[:, bass.ds(Q * p + q, 1), :]).then_inc(hp_copied, 1)
                    nc.gpsimd.tensor_copy(hp_lo[:, q:q + 1, :], h_lo[:, bass.ds(Q * p + q, 1), :]).then_inc(hp_copied, 1)

            copy_panel_h(0)
            with pool.Fori(1, PANELS) as p:
                copy_panel_h(p)

        @block.tensor
        def _(pe):
            def transpose(q, b, t):
                return nc.tensor.transpose(tr[q % RING][:, P * t:P * t + P], raw[:, b % RAW, t, P * q:P * q + P],
                                           ident[:, :])

            def wait_transpose(p, b, q):
                wait(pe, col_lo_done, UP * p + Q * b + q - RING + 1)
                if q == 0:
                    pe.wait_ge(raw_loaded[b % RAW], 16 * (BLOCKS // RAW * p + b // RAW + 1))

            def project(rhs, lhs):
                for q in range(Q):
                    last = nc.tensor.matmul(proj[:, P * q:P * q + P], lhs[:, P * q:P * q + P], rhs[:, :],
                                            start=True, stop=True)
                last.then_inc(proj_ready, 1)

            def project_panel(p, used):
                pe.wait_ge(out1_copied, p + 1)
                wait(pe, proj_used, used)
                project(w_in_sb, out1_sb)

            def project_chunk(c, used):
                pe.wait_ge(acc2_added, BLOCKS * LAST + c + 1)
                pe.wait_ge(proj_used, used)
                project(w_out_sb, acc2[:, BW * c:BW * c + BW])

            def multiply_blocks(p, first=False, last=False):
                for b in range(BLOCKS):
                    if not first and b == 1:
                        project_panel(p - 1, p - 1)
                    if last and b >= 2:
                        project_chunk(b - 2, PANELS - 1 + b - 2)
                    for q in range(Q):
                        unit = UP * p + Q * b + q
                        ahead = Q * b + q + AHEAD
                        transposes = not last or ahead < UP
                        if transposes:
                            ap, ab, aq = (p, ahead // Q, ahead % Q) if ahead < UP else (p + 1, 0, ahead - UP)
                            wait_transpose(ap, ab, aq)
                            transpose(aq, ab, 0)
                        pe.wait_ge(row_lo_done, unit + 1)
                        if b == 0:
                            pe.wait_ge(hp_copied, 2 * (Q * p + q + 1))
                        if q == 0:
                            wait(pe, acc2_added, BLOCKS * p + b - 1)
                        slot = q % RING
                        o2 = out2[b % 2][:, :]
                        nc.tensor.matmul(o2, hp_hi[:, q, :], row_hi[:, slot, :], start=q == 0, stop=False)
                        if transposes:
                            transpose(aq, ab, 1)
                        nc.tensor.matmul(o2, hp_hi[:, q, :], row_lo[:, slot, :], start=False, stop=False)
                        if transposes:
                            transpose(aq, ab, 2)
                        nc.tensor.matmul(o2, hp_lo[:, q, :], row_hi[:, slot, :], start=False,
                                         stop=q == Q - 1).then_inc(row_used, 1)
                        if transposes:
                            transpose(aq, ab, 3).then_inc(transposed, 1)
                        pe.wait_ge(col_lo_done, unit + 1)
                        if b == 0 and q == 0:
                            wait(pe, out1_copied, p)
                        if first and q == 0:
                            pe.wait_ge(chunk_h, b + 1)
                        t = Q * b + q
                        o1 = out1[:, :]
                        nc.tensor.matmul(o1, h_hi[:, t, :], col_hi[:, slot, :], start=t == 0, stop=False)
                        nc.tensor.matmul(o1, h_hi[:, t, :], col_lo[:, slot, :], start=False, stop=False)
                        nc.tensor.matmul(o1, h_lo[:, t, :], col_hi[:, slot, :], start=False,
                                         stop=t == TILES - 1).then_inc(col_used, 1)

            pe.wait_ge(ident_ready, 1)
            pe.wait_ge(w_loaded, 32)
            for q in range(AHEAD):
                wait_transpose(0, 0, q)
                for t in range(Q - 1):
                    transpose(q, 0, t)
                transpose(q, 0, Q - 1).then_inc(transposed, 1)
            multiply_blocks(0, first=True)
            with pe.Fori(1, LAST) as p:
                multiply_blocks(p)
            multiply_blocks(LAST, last=True)
            project_chunk(BLOCKS - 2, PANELS - 1 + BLOCKS - 2)
            project_panel(LAST, PANELS - 1 + BLOCKS - 1)
            project_chunk(BLOCKS - 1, PANELS + BLOCKS - 1)

        @block.scalar
        def _(act):
            act.dma_start(w_in_sb[:, :], w_in).then_inc(w_loaded, 16)
            act.dma_start(w_out_sb[:, :], w_out).then_inc(w_loaded, 16)

            def chunk_sqrt(c):
                act.wait_ge(chunk_var, c + 1)
                tiles = slice(Q * c, Q * c + Q)
                nc.scalar.activation(std[:, tiles], var_eps[:, tiles], ACT.Sqrt).then_inc(chunk_std, 1)

            def chunk_relu(c):
                act.wait_ge(chunk_norm, c + 1)
                nc.scalar.activation(h_hi[:, Q * c:Q * c + Q, :], norm, ACT.Relu).then_inc(chunk_hi, 1)

            def split_units(p, first=False):
                for b in range(BLOCKS):
                    for q in range(Q):
                        unit = UP * p + Q * b + q
                        slot = q % RING
                        if q == 0:
                            act.wait_ge(raw_loaded[b % RAW], 16 * (BLOCKS // RAW * p + b // RAW + 1))
                        if b == 0 and q == 0:
                            wait(act, rowsum_read, p)
                        wait(act, row_used, unit - RING + 1)
                        nc.scalar.activation(row_hi[:, slot, :], raw[:, b % RAW, q, :], ACT.Copy,
                                             accum_out=rowsum[:, q, b:b + 1]).then_inc(row_hi_done, 1)
                        act.wait_ge(transposed, unit + 1)
                        wait(act, col_used, unit - RING + 1)
                        t = Q * b + q
                        nc.scalar.activation(col_hi[:, slot, :], tr[slot][:, :], ACT.Copy,
                                             accum_out=colsum[:, t, bass.ds(p, 1)]).then_inc(col_hi_done, 1)
                        if first and q == 1 and b + 2 < BLOCKS:
                            chunk_sqrt(b + 2)
                        if first and q == 2 and b + 1 < BLOCKS:
                            chunk_relu(b + 1)
                        if not first and b == 0 and q == 1:
                            copy_out1(p - 1)

            def copy_out1(p):
                act.wait_ge(col_used, UP * p + UP)
                wait(act, proj_ready, p)
                nc.scalar.activation(out1_sb[:, :], out1[:, :], ACT.Copy).then_inc(out1_copied, 1)

            chunk_sqrt(0)
            chunk_relu(0)
            chunk_sqrt(1)
            split_units(0, first=True)
            with act.Fori(1, PANELS) as p:
                split_units(p)
            copy_out1(LAST)

        @block.vector
        def _(dve):
            def chunk_stats(c):
                tiles = slice(Q * c, Q * c + Q)
                dve.wait_ge(x_loaded[c], 16)
                for q in range(Q):
                    nc.vector.bn_stats(stats[:, q, :], xy[:, Q * c + q, :]).then_inc(h_step, 1)
                dve.wait_ge(h_step, H_STEPS * c + Q)
                for q in range(Q):
                    nc.vector.bn_aggr(mean_var[:, Q * c + q, :], stats[:, q, :]).then_inc(h_step, 1)
                dve.wait_ge(h_step, H_STEPS * c + 2 * Q)
                nc.vector.tensor_scalar(var_eps[:, tiles], mean_var[:, tiles, 1], LN_EPS, None,
                                        ALU.add).then_inc(chunk_var, 1)

            def chunk_normalise(c):
                tiles = slice(Q * c, Q * c + Q)
                dve.wait_ge(chunk_std, c + 1)
                steps = N_STEPS * c
                nc.vector.reciprocal(rstd[:, tiles], std[:, tiles]).then_inc(norm_step, 1)
                dve.wait_ge(norm_step, steps + 1)
                nc.vector.tensor_tensor(tmp[:, :], rstd[:, tiles], rstd[:, tiles], ALU.mult).then_inc(norm_step, 1)
                dve.wait_ge(norm_step, steps + 2)
                nc.vector.tensor_tensor(tmp2[:, :], tmp[:, :], var_eps[:, tiles], ALU.mult).then_inc(norm_step, 1)
                dve.wait_ge(norm_step, steps + 3)
                nc.vector.tensor_scalar(tmp[:, :], tmp2[:, :], -0.5, 1.5, ALU.mult, ALU.add).then_inc(norm_step, 1)
                dve.wait_ge(norm_step, steps + 4)
                nc.vector.tensor_tensor(tmp2[:, :], rstd[:, tiles], tmp[:, :], ALU.mult).then_inc(norm_step, 1)
                dve.wait_ge(norm_step, steps + 5)
                for q in range(Q):
                    last = nc.vector.tensor_scalar(norm[:, q, :], xy[:, Q * c + q, :], mean_var[:, Q * c + q, 0:1],
                                                   tmp2[:, q:q + 1], ALU.subtract, ALU.mult)
                last.then_inc(chunk_norm, 1)

            def chunk_low(c):
                tiles = slice(Q * c, Q * c + Q)
                dve.wait_ge(chunk_hi, c + 1)
                nc.vector.scalar_tensor_tensor(h_lo[:, tiles, :], norm, 0.0, h_hi[:, tiles, :].bitcast(F32),
                                               ALU.max, ALU.subtract).then_inc(chunk_h, 1)

            def add_out2(p, b):
                dve.wait_ge(row_used, UP * p + Q * b + Q)
                if b == 0 and isinstance(p, int) and p == 0:
                    dve.wait_ge(acc2_zeroed, 1)
                cols = slice(BW * b, BW * b + BW)
                nc.vector.tensor_tensor(acc2[:, cols], out2[b % 2][:, :], acc2[:, cols],
                                        ALU.add).then_inc(acc2_added, 1)

            def guard(deg, step, count):
                nc.vector.tensor_scalar(tmp[:, :], deg, 0.0, None, ALU.max).then_inc(step, 1)
                dve.wait_ge(step, count + 1)
                nc.vector.scalar_tensor_tensor(tmp2[:, :], deg, 0.0, tmp[:, :], ALU.is_le, ALU.add).then_inc(step, 1)
                dve.wait_ge(step, count + 2)
                nc.vector.reciprocal(rdeg[:, :], tmp2[:, :]).then_inc(step, 1)
                dve.wait_ge(step, count + 3)

            def sum_rows():
                nc.vector.tensor_reduce(row_deg[:, :], rowsum[:, :, :], AX.X, ALU.add).then_inc(rowsum_read, 1)

            def finish_rows(p, uses):
                dve.wait_ge(rowsum_read, p + 1)
                guard(row_deg[:, :], row_step, 3 * p)
                dve.wait_ge(proj_ready, uses + 1)
                for q in range(Q):
                    tile = xy[:, bass.ds(Q * p + q, 1), :]
                    part = proj[:, P * q:P * q + P].rearrange("p (a d) -> p a d", a=1)
                    last = nc.vector.scalar_tensor_tensor(tile, part, rdeg[:, q:q + 1], tile, ALU.mult, ALU.add)
                last.then_inc(proj_used, 1)

            def finish_chunk(c, uses):
                dve.wait_ge(col_hi_done, UP * LAST + Q * c + Q)
                nc.vector.tensor_reduce(col_deg[:, :], colsum[:, Q * c:Q * c + Q, :], AX.X, ALU.add).then_inc(col_step, 1)
                dve.wait_ge(col_step, 4 * c + 1)
                guard(col_deg[:, :], col_step, 4 * c + 1)
                dve.wait_ge(proj_ready, uses + 1)
                dve.wait_ge(proj_used, uses)
                for q in range(Q):
                    tile = xy[:, Q * c + q, :]
                    last = nc.vector.scalar_tensor_tensor(tile, proj[:, P * q:P * q + P], rdeg[:, q:q + 1], tile,
                                                          ALU.mult, ALU.add)
                last.then_inc(proj_used, 1)

            def split_units(p, first=False, last=False):
                for b in range(BLOCKS):
                    for q in range(Q):
                        unit = UP * p + Q * b + q
                        slot = q % RING
                        dve.wait_ge(row_hi_done, unit + 1)
                        nc.vector.tensor_tensor(row_lo[:, slot, :], raw[:, b % RAW, q, :],
                                                row_hi[:, slot, :].bitcast(F32), ALU.subtract).then_inc(row_lo_done, 1)
                        dve.wait_ge(col_hi_done, unit + 1)
                        nc.vector.tensor_tensor(col_lo[:, slot, :], tr[slot][:, :],
                                                col_hi[:, slot, :].bitcast(F32), ALU.subtract).then_inc(col_lo_done, 1)
                        if q == 1 and b > 0:
                            add_out2(p, b - 1)
                        if q == 1 and b == 0 and not first:
                            add_out2(p - 1, BLOCKS - 1)
                        if first:
                            if q == 0 and b + 2 < BLOCKS:
                                chunk_stats(b + 2)
                            if q == 1 and b + 1 < BLOCKS:
                                chunk_normalise(b + 1)
                            if q == 3 and b + 1 < BLOCKS:
                                chunk_low(b + 1)
                        elif b == 1 and q == 3:
                            finish_rows(p - 1, p - 1)
                        if last and b >= 2 and q == 3:
                            finish_chunk(b - 2, LAST + b - 2)
                sum_rows()

            chunk_stats(0)
            chunk_normalise(0)
            chunk_low(0)
            chunk_stats(1)
            split_units(0, first=True)
            with dve.Fori(1, LAST) as p:
                split_units(p)
            split_units(LAST, last=True)
            add_out2(LAST, BLOCKS - 1)
            finish_chunk(BLOCKS - 2, LAST + BLOCKS - 2)
            finish_rows(LAST, LAST + BLOCKS - 1)
            finish_chunk(BLOCKS - 1, LAST + BLOCKS)


def kernel(**inputs):
    import numpy as _np
    import concourse.bacc as _bacc
    from concourse import mybir as _mybir
    from concourse.bass_utils import run_bass_kernel_spmd as _run

    nc = _bacc.Bacc("TRN2", target_bir_lowering=False, num_devices=1)
    arrays, args = {}, []
    for name in ("x", "adj", "L0_gnn_W_in", "L0_gnn_W_out"):
        a = _np.ascontiguousarray(inputs[name])
        arrays[f"in_{name}"] = a
        args.append(nc.dram_tensor(f"in_{name}", a.shape, _mybir.dt.from_np(a.dtype), kind="ExternalInput").ap())
    shape = inputs["x"].shape
    args.append(nc.dram_tensor("out_0", shape, _mybir.dt.float32, kind="ExternalOutput").ap())
    gnn_layer_kernel(nc, *args)
    r = _run(nc, [arrays], core_ids=[0])
    return r.results[0]["out_0"]
```

```python
from contextlib import ExitStack

import concourse.bass as bass
from concourse import mybir

P = 128
S = 32
LN_EPS = 1e-5


def gnn_layer_kernel(nc: bass.Bass, x: bass.AP, adj: bass.AP, w_in: bass.AP, w_out: bass.AP, out: bass.AP):
    F32 = mybir.dt.float32
    F32R = mybir.dt.float32r
    ALU = mybir.AluOpType
    ACT = mybir.ActivationFunctionType
    AX = mybir.AxisListType

    N, D = x.shape
    Q = 4
    BW = Q * P
    PANELS = N // BW
    BLOCKS = N // BW
    PAIRS = BLOCKS // 2
    TILES = N // P
    UNITS = Q * BLOCKS
    HALF = UNITS // 2
    PAIR = 2 * Q
    BUFS = 2
    RING = 4
    AHEAD = 2
    LAST = PANELS - 1
    H_STEPS = 2 * Q
    N_STEPS = 5
    assert D == P and PANELS == BLOCKS and PAIRS % BUFS == 0 and UNITS % RING == 0

    x_chunks = x.rearrange("(k p c) d -> k p (c d)", p=P, c=Q)
    out_chunks = out.rearrange("(k p c) d -> k p (c d)", p=P, c=Q)
    adj_panels = adj.rearrange("(n p c) j -> n p c j", p=P, c=Q)
    adj_squares = adj.rearrange("(n i r) j -> n r i j", i=BW // S, r=S)
    y_dram = nc.dram_tensor("y_rows", [PANELS, P, Q * D], F32, kind="Internal").ap()

    ctx = ExitStack()
    with ctx:
        def sb(name, shape, dt=F32):
            return ctx.enter_context(nc.sbuf_tensor(name, shape, dt))

        def pb(name):
            return ctx.enter_context(nc.psum_tensor(name, [P, BW], F32))

        def sem(name):
            return ctx.enter_context(nc.semaphore(name))

        h_hi = sb("h_hi", [P, TILES, D], F32R)
        h_lo = sb("h_lo", [P, TILES, D], F32R)
        acc2 = sb("acc2", [P, N])
        w_in_sb = sb("w_in_sb", [P, D])
        w_out_sb = sb("w_out_sb", [P, D])
        ident = sb("ident", [P, P])
        colsum = sb("colsum", [P, TILES, PANELS])
        rowsum = sb("rowsum", [P, Q, BLOCKS])

        even = sb("even", [P, BUFS, Q, BW])
        odd = sb("odd", [P, BUFS, Q, BW])
        squares = sb("squares", [P, BUFS, BW // S, P])
        col_t = sb("col_t", [P, 2, BW])
        row_hi = sb("row_hi", [P, RING, BW], F32R)
        row_lo = sb("row_lo", [P, RING, BW], F32R)
        col_hi = sb("col_hi", [P, RING, BW], F32R)
        col_lo = sb("col_lo", [P, RING, BW], F32R)
        hp_hi = sb("hp_hi", [P, Q, D], F32R)
        hp_lo = sb("hp_lo", [P, Q, D], F32R)
        chunk = sb("chunk", [P, 2, Q, D])
        rows = sb("rows", [P, Q, D])
        out1_sb = sb("out1_sb", [P, BW])
        stats = sb("stats", [P, Q, 6])
        mean_var = sb("mean_var", [P, TILES, 2])
        var_eps = sb("var_eps", [P, TILES])
        std = sb("std", [P, TILES])
        rstd = sb("rstd", [P, TILES])
        tmp = sb("tmp", [P, Q])
        tmp2 = sb("tmp2", [P, Q])
        row_deg = sb("row_deg", [P, Q])
        col_deg = sb("col_deg", [P, Q])
        rdeg = sb("rdeg", [P, Q])
        norm = out1_sb[:, :].rearrange("p (q d) -> p q d", q=Q)

        tr = [pb("tr0"), pb("tr1")]
        out2 = [pb("out2a"), pb("out2b")]
        out1 = pb("out1")
        proj = pb("proj")

        x_loaded = [sem("x_loaded0"), sem("x_loaded1")]
        w_loaded = sem("w_loaded")
        even_loaded = [sem("even_loaded0"), sem("even_loaded1")]
        odd_loaded = [sem("odd_loaded0"), sem("odd_loaded1")]
        squares_loaded = [sem("squares_loaded0"), sem("squares_loaded1")]
        rows_loaded = sem("rows_loaded")
        y_stored = sem("y_stored")
        y_loaded = [sem("y_loaded0"), sem("y_loaded1")]
        out_stored = [sem("out_stored0"), sem("out_stored1")]
        ident_zeroed = sem("ident_zeroed")
        ident_ready = sem("ident_ready")
        acc2_zeroed = sem("acc2_zeroed")
        chunk_var = sem("chunk_var")
        chunk_std = sem("chunk_std")
        chunk_norm = sem("chunk_norm")
        chunk_hi = sem("chunk_hi")
        chunk_h = sem("chunk_h")
        hp_copied = sem("hp_copied")
        transposed = sem("transposed")
        col_t_done = sem("col_t_done")
        row_hi_done = sem("row_hi_done")
        row_lo_dve = sem("row_lo_dve")
        row_lo_pool = sem("row_lo_pool")
        col_hi_done = sem("col_hi_done")
        col_lo_done = sem("col_lo_done")
        row_used = sem("row_used")
        col_used = sem("col_used")
        acc2_added = sem("acc2_added")
        out1_copied = sem("out1_copied")
        proj_ready = sem("proj_ready")
        proj_used = sem("proj_used")
        rowsum_read = sem("rowsum_read")
        h_step, norm_step, row_step, col_step = sem("h_step"), sem("norm_step"), sem("row_step"), sem("col_step")

        block = ctx.enter_context(nc.Block())

        def wait(eng, semaphore, value):
            if not isinstance(value, int) or value > 0:
                eng.wait_ge(semaphore, value)

        def first_panel(p):
            return isinstance(p, int) and p == 0

        def on_pool(p, k):
            return first_panel(p) or k % 2 == 1

        def row_lo_count(p, k):
            if first_panel(p):
                return k + 1
            return HALF * (p + 1 if on_pool(p, k) else p - 1) + k // 2 + 1

        def loads_of_slot(p, m):
            return PAIRS // BUFS * p + m // BUFS + 1

        def row_tile(k):
            source = even if k % PAIR < Q else odd
            return source[:, k // PAIR % BUFS, k % Q, :]

        def col_tile(k):
            return 2 * (k // PAIR) + k % 2, k % PAIR // 2

        def tile_columns(cols, c):
            return cols.rearrange("p (i c) -> p c i", c=Q)[:, c]

        @block.sync
        def _(sp):
            def load_pairs(p):
                for m in range(PAIRS):
                    slot = m % BUFS
                    before = UNITS * p + PAIR * (m - BUFS)
                    col = 2 * m * BW
                    wait(sp, col_used, before + Q + 1)
                    sp.dma_start(even[:, slot], adj_panels[p][:, :, col:col + BW]).then_inc(even_loaded[slot], 16)
                    wait(sp, col_used, before + PAIR - 1)
                    for a in range(Q):
                        quad = col + BW + P * a
                        sp.dma_start(squares[S * a:S * a + S, slot], adj_squares[p][:, :, quad:quad + P]
                                     ).then_inc(squares_loaded[slot], 16)
                    wait(sp, col_used, before + PAIR)
                    sp.dma_start(odd[:, slot], adj_panels[p][:, :, col + BW:col + 2 * BW]
                                 ).then_inc(odd_loaded[slot], 16)

            load_pairs(0)
            with sp.Fori(1, PANELS) as p:
                load_pairs(p)

        @block.gpsimd
        def _(pool):
            nc.gpsimd.memset(ident[:, :], 0.0).then_inc(ident_zeroed, 1)
            pool.wait_ge(ident_zeroed, 1)
            nc.gpsimd.affine_select(out=ident[:, :], in_=ident[:, :], compare_op=ALU.not_equal, fill=1.0, base=0,
                                    pattern=[[-1, P]], channel_multiplier=1).then_inc(ident_ready, 1)
            nc.gpsimd.memset(acc2[:, :], 0.0).then_inc(acc2_zeroed, 1)

            def split_units(p):
                for k in range(UNITS):
                    if on_pool(p, k):
                        pool.wait_ge(row_hi_done, UNITS * p + k + 1)
                        nc.gpsimd.tensor_tensor(row_lo[:, k % RING, :], row_tile(k),
                                                row_hi[:, k % RING, :].bitcast(F32), ALU.subtract
                                                ).then_inc(row_lo_pool, 1)

            split_units(0)
            with pool.Fori(1, PANELS) as p:
                split_units(p)

        @block.tensor
        def _(pe):
            def transpose(k, t):
                source = even[:, k // PAIR % BUFS, t, :]
                return nc.tensor.transpose(tr[k // 2 % 2][:, P * t:P * t + P], tile_columns(source, col_tile(k)[1]),
                                           ident[:, :])

            def wait_transpose(p, k):
                wait(pe, col_lo_done, UNITS * p + k - 3)
                if k % PAIR == 0:
                    pe.wait_ge(even_loaded[k // PAIR % BUFS], 16 * loads_of_slot(p, k // PAIR))

            def project_panel(p, used):
                pe.wait_ge(out1_copied, p + 1)
                wait(pe, proj_used, used)
                for q in range(Q):
                    last = nc.tensor.matmul(proj[:, P * q:P * q + P], out1_sb[:, P * q:P * q + P], w_in_sb[:, :],
                                            start=True, stop=True)
                last.then_inc(proj_ready, 1)

            def project_chunk(c, used):
                pe.wait_ge(acc2_added, BLOCKS * LAST + c + 1)
                pe.wait_ge(proj_used, used)
                for q in range(Q):
                    last = nc.tensor.matmul(proj[:, P * q:P * q + P], tile_columns(acc2[:, BW * c:BW * c + BW], q),
                                            w_out_sb[:, :], start=True, stop=True)
                last.then_inc(proj_ready, 1)

            def multiply_units(p, last=False):
                first = first_panel(p)
                for k in range(UNITS):
                    unit = UNITS * p + k
                    b, q, slot = k // Q, k % Q, k % RING
                    if k == Q and not first:
                        project_panel(p - 1, p - 1)
                    if q == 0 and last and b >= 2:
                        project_chunk(b - 2, LAST + b - 2)
                    ahead = k + AHEAD
                    transposes = k % 2 == 0 and not (last and ahead >= UNITS)
                    if transposes:
                        wait_transpose(*((p, ahead) if ahead < UNITS else (p + 1, ahead - UNITS)))
                        transpose(ahead % UNITS, 0)
                    if on_pool(p, k):
                        pe.wait_ge(row_lo_pool, row_lo_count(p, k))
                    else:
                        pe.wait_ge(row_lo_dve, row_lo_count(p, k))
                    if b == 0:
                        pe.wait_ge(hp_copied, 2 * (Q * p + q + 1))
                    if q == 0:
                        wait(pe, acc2_added, BLOCKS * p + b - 1)
                    o2 = out2[b % 2][:, :]
                    nc.tensor.matmul(o2, hp_hi[:, q, :], row_hi[:, slot, :], start=q == 0, stop=False)
                    if transposes:
                        transpose(ahead % UNITS, 1)
                    nc.tensor.matmul(o2, hp_hi[:, q, :], row_lo[:, slot, :], start=False, stop=False)
                    if transposes:
                        transpose(ahead % UNITS, 2)
                    nc.tensor.matmul(o2, hp_lo[:, q, :], row_hi[:, slot, :], start=False,
                                     stop=q == Q - 1).then_inc(row_used, 1)
                    if transposes:
                        transpose(ahead % UNITS, 3).then_inc(transposed, 1)
                    pe.wait_ge(col_lo_done, unit + 1)
                    if k == 0:
                        wait(pe, out1_copied, p)
                    c, tile = col_tile(k)
                    t = Q * c + tile
                    if first:
                        pe.wait_ge(chunk_h, c + 1)
                    o1 = out1[:, :]
                    nc.tensor.matmul(o1, h_hi[:, t, :], col_hi[:, slot, :], start=k == 0, stop=False)
                    nc.tensor.matmul(o1, h_hi[:, t, :], col_lo[:, slot, :], start=False, stop=False)
                    nc.tensor.matmul(o1, h_lo[:, t, :], col_hi[:, slot, :], start=False,
                                     stop=k == UNITS - 1).then_inc(col_used, 1)

            pe.wait_ge(ident_ready, 1)
            pe.wait_ge(w_loaded, 32)
            wait_transpose(0, 0)
            for t in range(Q - 1):
                transpose(0, t)
            transpose(0, Q - 1).then_inc(transposed, 1)
            multiply_units(0)
            with pe.Fori(1, LAST) as p:
                multiply_units(p)
            multiply_units(LAST, last=True)
            project_chunk(BLOCKS - 2, LAST + BLOCKS - 2)
            project_panel(LAST, LAST + BLOCKS - 1)
            project_chunk(BLOCKS - 1, LAST + BLOCKS)

        @block.scalar
        def _(act):
            def flat(tiles):
                return tiles.rearrange("p q d -> p (q d)")

            def load_x(c):
                wait(act, chunk_norm, c - 1)
                act.dma_start(flat(chunk[:, c % 2]), x_chunks[c]).then_inc(x_loaded[c % 2], 16)

            def load_rows(p):
                wait(act, y_stored, 16 * p)
                act.dma_start(flat(rows[:, :, :]), x_chunks[p]).then_inc(rows_loaded, 16)

            def store_y(p):
                act.wait_ge(proj_used, p + 1)
                act.dma_start(y_dram[p], flat(rows[:, :, :])).then_inc(y_stored, 16)

            def load_y(c):
                wait(act, out_stored[c % 2], 16 * (c // 2))
                act.dma_start(flat(chunk[:, c % 2]), y_dram[c]).then_inc(y_loaded[c % 2], 16)

            def store_out(c):
                act.wait_ge(proj_used, LAST + c + 1 if c < BLOCKS - 1 else PANELS + BLOCKS)
                done = chunk[:, c % 2] if c < BLOCKS - 1 else rows[:, :, :]
                act.dma_start(out_chunks[c], flat(done)).then_inc(out_stored[c % 2], 16)

            def chunk_sqrt(c):
                tiles = slice(Q * c, Q * c + Q)
                act.wait_ge(chunk_var, c + 1)
                nc.scalar.activation(std[:, tiles], var_eps[:, tiles], ACT.Sqrt).then_inc(chunk_std, 1)

            def chunk_relu(c):
                act.wait_ge(chunk_norm, c + 1)
                nc.scalar.activation(h_hi[:, Q * c:Q * c + Q, :], norm, ACT.Relu).then_inc(chunk_hi, 1)

            def copy_out1(p):
                act.wait_ge(col_used, UNITS * p + UNITS)
                wait(act, proj_ready, p)
                nc.scalar.activation(out1_sb[:, :], out1[:, :], ACT.Copy).then_inc(out1_copied, 1)

            def split_units(p, last=False):
                first = first_panel(p)
                for k in range(UNITS):
                    unit = UNITS * p + k
                    b, q, slot, m = k // Q, k % Q, k % RING, k // PAIR
                    if q == 0:
                        loaded = (even_loaded, odd_loaded)[b % 2][m % BUFS]
                        act.wait_ge(loaded, 16 * loads_of_slot(p, m))
                    if k == 0:
                        wait(act, rowsum_read, p)
                    wait(act, row_used, unit - RING + 1)
                    nc.scalar.activation(row_hi[:, slot, :], row_tile(k), ACT.Copy,
                                         accum_out=rowsum[:, q, b:b + 1]).then_inc(row_hi_done, 1)
                    if k % 2 == 0:
                        act.wait_ge(transposed, HALF * p + k // 2 + 1)
                        source = tr[k // 2 % 2][:, :]
                    else:
                        act.wait_ge(col_t_done, HALF * p + k // 2 + 1)
                        source = col_t[:, k // 2 % 2, :]
                    wait(act, col_used, unit - RING + 1)
                    c, tile = col_tile(k)
                    nc.scalar.activation(col_hi[:, slot, :], source, ACT.Copy,
                                         accum_out=colsum[:, Q * c + tile, bass.ds(p, 1)]).then_inc(col_hi_done, 1)
                    if first:
                        if q == 2 and b + 2 < BLOCKS:
                            chunk_relu(b + 2)
                        if q == 2 and b + 4 < BLOCKS:
                            load_x(b + 4)
                        if q == 3 and b + 3 < BLOCKS:
                            chunk_sqrt(b + 3)
                    else:
                        if k == 1:
                            copy_out1(p - 1)
                        if b == 3 and q == 0:
                            store_y(p - 1)
                        if b == 5 and q == 0:
                            load_rows(p)
                    if last:
                        if b == 0 and q == 2:
                            load_y(0)
                            load_y(1)
                        if b >= 3 and q == 1:
                            store_out(b - 3)
                        if b >= 3 and q == 3:
                            load_y(b - 1)

            load_x(0)
            load_x(1)
            act.dma_start(w_in_sb[:, :], w_in).then_inc(w_loaded, 16)
            act.dma_start(w_out_sb[:, :], w_out).then_inc(w_loaded, 16)
            load_rows(0)
            for c in range(2):
                chunk_sqrt(c)
                chunk_relu(c)
                load_x(c + 2)
            chunk_sqrt(2)
            split_units(0)
            with act.Fori(1, LAST) as p:
                split_units(p)
            split_units(LAST, last=True)
            copy_out1(LAST)
            for c in range(BLOCKS - 3, BLOCKS):
                store_out(c)
            act.wait_ge(out_stored[0], 16 * BLOCKS // 2)
            act.wait_ge(out_stored[1], 16 * BLOCKS // 2)
            act.wait_ge(y_stored, 16 * LAST)

        @block.vector
        def _(dve):
            def chunk_stats(c):
                tiles = slice(Q * c, Q * c + Q)
                dve.wait_ge(x_loaded[c % 2], 16 * (c // 2 + 1))
                for q in range(Q):
                    nc.vector.bn_stats(stats[:, q, :], chunk[:, c % 2, q, :]).then_inc(h_step, 1)
                dve.wait_ge(h_step, H_STEPS * c + Q)
                for q in range(Q):
                    nc.vector.bn_aggr(mean_var[:, Q * c + q, :], stats[:, q, :]).then_inc(h_step, 1)
                dve.wait_ge(h_step, H_STEPS * c + 2 * Q)
                nc.vector.tensor_scalar(var_eps[:, tiles], mean_var[:, tiles, 1], LN_EPS, None,
                                        ALU.add).then_inc(chunk_var, 1)

            def chunk_normalise(c):
                tiles = slice(Q * c, Q * c + Q)
                dve.wait_ge(chunk_std, c + 1)
                steps = N_STEPS * c
                nc.vector.reciprocal(rstd[:, tiles], std[:, tiles]).then_inc(norm_step, 1)
                dve.wait_ge(norm_step, steps + 1)
                nc.vector.tensor_tensor(tmp[:, :], rstd[:, tiles], rstd[:, tiles], ALU.mult).then_inc(norm_step, 1)
                dve.wait_ge(norm_step, steps + 2)
                nc.vector.tensor_tensor(tmp2[:, :], tmp[:, :], var_eps[:, tiles], ALU.mult).then_inc(norm_step, 1)
                dve.wait_ge(norm_step, steps + 3)
                nc.vector.tensor_scalar(tmp[:, :], tmp2[:, :], -0.5, 1.5, ALU.mult, ALU.add).then_inc(norm_step, 1)
                dve.wait_ge(norm_step, steps + 4)
                nc.vector.tensor_tensor(tmp2[:, :], rstd[:, tiles], tmp[:, :], ALU.mult).then_inc(norm_step, 1)
                dve.wait_ge(norm_step, steps + 5)
                for q in range(Q):
                    last = nc.vector.tensor_scalar(norm[:, q, :], chunk[:, c % 2, q, :], mean_var[:, Q * c + q, 0:1],
                                                   tmp2[:, q:q + 1], ALU.subtract, ALU.mult)
                last.then_inc(chunk_norm, 1)

            def chunk_low(c):
                tiles = slice(Q * c, Q * c + Q)
                dve.wait_ge(chunk_hi, c + 1)
                nc.vector.scalar_tensor_tensor(h_lo[:, tiles, :], norm, 0.0, h_hi[:, tiles, :].bitcast(F32),
                                               ALU.max, ALU.subtract).then_inc(chunk_h, 1)

            def add_out2(p, b):
                dve.wait_ge(row_used, UNITS * p + Q * b + Q)
                if b == 0 and first_panel(p):
                    dve.wait_ge(acc2_zeroed, 1)
                cols = slice(BW * b, BW * b + BW)
                nc.vector.tensor_tensor(acc2[:, cols], out2[b % 2][:, :], acc2[:, cols],
                                        ALU.add).then_inc(acc2_added, 1)

            def guard(deg, step, count):
                nc.vector.tensor_scalar(tmp[:, :], deg, 0.0, None, ALU.max).then_inc(step, 1)
                dve.wait_ge(step, count + 1)
                nc.vector.scalar_tensor_tensor(tmp2[:, :], deg, 0.0, tmp[:, :], ALU.is_le, ALU.add).then_inc(step, 1)
                dve.wait_ge(step, count + 2)
                nc.vector.reciprocal(rdeg[:, :], tmp2[:, :]).then_inc(step, 1)
                dve.wait_ge(step, count + 3)

            def sum_rows():
                nc.vector.tensor_reduce(row_deg[:, :], rowsum[:, :, :], AX.X, ALU.add).then_inc(rowsum_read, 1)

            def finish_rows(p, uses):
                dve.wait_ge(rows_loaded, 16 * (p + 1))
                dve.wait_ge(rowsum_read, p + 1)
                guard(row_deg[:, :], row_step, 3 * p)
                dve.wait_ge(proj_ready, uses + 1)
                for q in range(Q):
                    last = nc.vector.scalar_tensor_tensor(rows[:, q, :], proj[:, P * q:P * q + P], rdeg[:, q:q + 1],
                                                          rows[:, q, :], ALU.mult, ALU.add)
                last.then_inc(proj_used, 1)

            def finish_chunk(c, uses):
                dve.wait_ge(col_hi_done, UNITS * LAST + PAIR * (c // 2 + 1))
                nc.vector.tensor_reduce(col_deg[:, :], colsum[:, Q * c:Q * c + Q, :], AX.X, ALU.add).then_inc(col_step, 1)
                dve.wait_ge(col_step, 4 * c + 1)
                guard(col_deg[:, :], col_step, 4 * c + 1)
                dve.wait_ge(proj_ready, uses + 1)
                if c < BLOCKS - 1:
                    dve.wait_ge(y_loaded[c % 2], 16 * (c // 2 + 1))
                else:
                    dve.wait_ge(proj_used, uses)
                for q in range(Q):
                    tile = chunk[:, c % 2, q, :] if c < BLOCKS - 1 else rows[:, q, :]
                    last = nc.vector.scalar_tensor_tensor(tile, proj[:, P * q:P * q + P], rdeg[:, q:q + 1], tile,
                                                          ALU.mult, ALU.add)
                last.then_inc(proj_used, 1)

            def copy_h(p, q):
                wait(dve, row_used, UNITS * p - Q + q + 1)
                dve.wait_ge(chunk_h, p + 1)
                nc.vector.tensor_copy(hp_hi[:, q:q + 1, :], h_hi[:, bass.ds(Q * p + q, 1), :]).then_inc(hp_copied, 1)
                nc.vector.tensor_copy(hp_lo[:, q:q + 1, :], h_lo[:, bass.ds(Q * p + q, 1), :]).then_inc(hp_copied, 1)

            def transpose_odd(p, k):
                slot = k // PAIR % BUFS
                if k % PAIR == 1:
                    dve.wait_ge(squares_loaded[slot], 16 * Q * loads_of_slot(p, k // PAIR))
                tile = squares[:, slot].rearrange("p i (s c) -> p c i s", c=Q)[:, col_tile(k)[1]]
                nc.vector.transpose(col_t[:, k // 2 % 2, :].rearrange("p (t m) -> p m t", t=Q),
                                    tile).then_inc(col_t_done, 1)

            def split_units(p, last=False):
                first = first_panel(p)
                for k in range(UNITS):
                    unit = UNITS * p + k
                    b, q, slot = k // Q, k % Q, k % RING
                    if k % 2 == 0:
                        wait(dve, col_hi_done, unit - 2)
                        wait(dve, col_lo_done, unit - 2)
                        transpose_odd(p, k + 1)
                    if b == 0:
                        copy_h(p, q)
                    if not on_pool(p, k):
                        dve.wait_ge(row_hi_done, unit + 1)
                        nc.vector.tensor_tensor(row_lo[:, slot, :], row_tile(k), row_hi[:, slot, :].bitcast(F32),
                                                ALU.subtract).then_inc(row_lo_dve, 1)
                    dve.wait_ge(col_hi_done, unit + 1)
                    source = tr[k // 2 % 2][:, :] if k % 2 == 0 else col_t[:, k // 2 % 2, :]
                    nc.vector.tensor_tensor(col_lo[:, slot, :], source, col_hi[:, slot, :].bitcast(F32),
                                            ALU.subtract).then_inc(col_lo_done, 1)
                    if q == 1 and b > 0:
                        add_out2(p, b - 1)
                    if k == 1 and not first:
                        add_out2(p - 1, BLOCKS - 1)
                    if first:
                        if q == 1 and b + 2 < BLOCKS:
                            chunk_normalise(b + 2)
                        if q == 2 and b + 3 < BLOCKS:
                            chunk_stats(b + 3)
                        if q == 3 and b + 2 < BLOCKS:
                            chunk_low(b + 2)
                    elif b == 1 and q == 3:
                        finish_rows(p - 1, p - 1)
                    if last and b >= 2 and q == 3:
                        finish_chunk(b - 2, LAST + b - 2)
                sum_rows()

            for c in range(2):
                chunk_stats(c)
                chunk_normalise(c)
                chunk_low(c)
            chunk_stats(2)
            split_units(0)
            with dve.Fori(1, LAST) as p:
                split_units(p)
            split_units(LAST, last=True)
            add_out2(LAST, BLOCKS - 1)
            finish_chunk(BLOCKS - 2, LAST + BLOCKS - 2)
            finish_rows(LAST, LAST + BLOCKS - 1)
            finish_chunk(BLOCKS - 1, LAST + BLOCKS)


def kernel(**inputs):
    import numpy as _np
    import concourse.bacc as _bacc
    from concourse import mybir as _mybir
    from concourse.bass_utils import run_bass_kernel_spmd as _run

    nc = _bacc.Bacc("TRN2", target_bir_lowering=False, num_devices=1)
    arrays, args = {}, []
    for name in ("x", "adj", "L0_gnn_W_in", "L0_gnn_W_out"):
        a = _np.ascontiguousarray(inputs[name])
        arrays[f"in_{name}"] = a
        args.append(nc.dram_tensor(f"in_{name}", a.shape, _mybir.dt.from_np(a.dtype), kind="ExternalInput").ap())
    shape = inputs["x"].shape
    args.append(nc.dram_tensor("out_0", shape, _mybir.dt.float32, kind="ExternalOutput").ap())
    gnn_layer_kernel(nc, *args)
    r = _run(nc, [arrays], core_ids=[0])
    return r.results[0]["out_0"]
```

```python
from contextlib import ExitStack

import concourse.bass as bass
from concourse import mybir

P = 128
S = 32
LN_EPS = 1e-5


def gnn_layer_kernel(nc: bass.Bass, x: bass.AP, adj: bass.AP, w_in: bass.AP, w_out: bass.AP, out: bass.AP):
    F32 = mybir.dt.float32
    F32R = mybir.dt.float32r
    ALU = mybir.AluOpType
    ACT = mybir.ActivationFunctionType
    AX = mybir.AxisListType

    N, D = x.shape
    Q = 4
    BW = Q * P
    PANELS = N // BW
    BLOCKS = N // BW
    PAIRS = BLOCKS // 2
    TILES = N // P
    UNITS = Q * BLOCKS
    HALF = UNITS // 2
    POOL_UNITS = HALF + Q
    PAIR = 2 * Q
    BUFS = 2
    RING = 4
    AHEAD = 2
    LAST = PANELS - 1
    X_GROUPS = [(0, 2), (2, 4), (4, 6), (6, 8), (8, 12), (12, BLOCKS)]
    assert D == P and PANELS == BLOCKS and PAIRS % BUFS == 0 and UNITS % RING == 0

    x_chunks = x.rearrange("(k p c) d -> k p (c d)", p=P, c=Q)
    out_chunks = out.rearrange("(k p c) d -> k p (c d)", p=P, c=Q)
    adj_panels = adj.rearrange("(n p c) j -> n p c j", p=P, c=Q)
    adj_squares = adj.rearrange("(n i r) j -> n r i j", i=BW // S, r=S)
    y_dram = nc.dram_tensor("y_rows", [PANELS, P, Q * D], F32, kind="Internal").ap()

    ctx = ExitStack()
    with ctx:
        def sb(name, shape, dt=F32):
            return ctx.enter_context(nc.sbuf_tensor(name, shape, dt))

        def pb(name):
            return ctx.enter_context(nc.psum_tensor(name, [P, BW], F32))

        def sem(name):
            return ctx.enter_context(nc.semaphore(name))

        h_hi = sb("h_hi", [P, TILES, D], F32R)
        h_lo = sb("h_lo", [P, TILES, D], F32R)
        acc2 = sb("acc2", [P, N])
        w_in_sb = sb("w_in_sb", [P, D])
        w_out_sb = sb("w_out_sb", [P, D])
        ident = sb("ident", [P, P])
        colsum = sb("colsum", [P, TILES, PANELS])
        rowsum = sb("rowsum", [P, Q, BLOCKS])

        even = sb("even", [P, BUFS, Q, BW])
        odd = sb("odd", [P, BUFS, Q, BW])
        squares = sb("squares", [P, BUFS, BW // S, P])
        col_t = sb("col_t", [P, 2, BW])
        row_hi = sb("row_hi", [P, RING, BW], F32R)
        row_lo = sb("row_lo", [P, RING, BW], F32R)
        col_hi = sb("col_hi", [P, RING, BW], F32R)
        col_lo = sb("col_lo", [P, RING, BW], F32R)
        hp_hi = sb("hp_hi", [P, Q, D], F32R)
        hp_lo = sb("hp_lo", [P, Q, D], F32R)
        chunk = sb("chunk", [P, 2, Q, D])
        rows = sb("rows", [P, Q, D])
        out1_sb = sb("out1_sb", [P, BW])
        stats = sb("stats", [P, 2 * Q, 6])
        mean_var = sb("mean_var", [P, TILES, 2])
        var_eps = sb("var_eps", [P, TILES])
        std = sb("std", [P, TILES])
        rstd = sb("rstd", [P, TILES])
        newton = sb("newton", [P, 2, 2 * Q])
        row_deg, row_max, row_safe, row_rdeg = (sb(n, [P, Q]) for n in ("row_deg", "row_max", "row_safe", "row_rdeg"))
        col_deg, col_max, col_safe, col_rdeg = (sb(n, [P, 2 * Q]) for n in ("col_deg", "col_max", "col_safe", "col_rdeg"))
        x_sb = acc2[:, :].rearrange("p (t d) -> p t d", d=D)

        tr = [pb("tr0"), pb("tr1")]
        out2 = [pb("out2a"), pb("out2b")]
        out1 = pb("out1")
        proj_rows = pb("proj_rows")
        proj_cols = [pb("proj_cols0"), pb("proj_cols1")]

        x_loaded = [sem(f"x_loaded{g}") for g in range(len(X_GROUPS))]
        w_loaded = sem("w_loaded")
        even_loaded = [sem("even_loaded0"), sem("even_loaded1")]
        odd_loaded = [sem("odd_loaded0"), sem("odd_loaded1")]
        squares_loaded = [sem("squares_loaded0"), sem("squares_loaded1")]
        rows_loaded = sem("rows_loaded")
        y_stored = sem("y_stored")
        y_loaded = [sem("y_loaded0"), sem("y_loaded1")]
        out_stored = [sem("out_stored0"), sem("out_stored1")]
        ident_zeroed = sem("ident_zeroed")
        ident_ready = sem("ident_ready")
        last_zeroed = sem("last_zeroed")
        var_done = sem("var_done")
        std_done = sem("std_done")
        norm_done = sem("norm_done")
        h_hi_done = sem("h_hi_done")
        h_done = sem("h_done")
        hp_copied = sem("hp_copied")
        transposed = sem("transposed")
        col_t_done = sem("col_t_done")
        row_hi_done = sem("row_hi_done")
        row_lo_dve = sem("row_lo_dve")
        row_lo_pool = sem("row_lo_pool")
        col_hi_done = sem("col_hi_done")
        col_lo_done = sem("col_lo_done")
        row_used = sem("row_used")
        col_used = sem("col_used")
        acc2_added = sem("acc2_added")
        out1_copied = sem("out1_copied")
        rows_projected = sem("rows_projected")
        rows_added = sem("rows_added")
        cols_projected = sem("cols_projected")
        cols_added = sem("cols_added")
        rowsum_read = sem("rowsum_read")
        stats_step, norm_step, row_step, col_step = (sem(n) for n in ("stats_step", "norm_step", "row_step", "col_step"))

        block = ctx.enter_context(nc.Block())

        def wait(eng, semaphore, value):
            if not isinstance(value, int) or value > 0:
                eng.wait_ge(semaphore, value)

        def first_panel(p):
            return isinstance(p, int) and p == 0

        def on_pool(p, k):
            return first_panel(p) or k % 2 == 1 or k < PAIR

        def row_lo_count(p, k):
            if first_panel(p):
                return k + 1
            before = sum(on_pool(None, other) == on_pool(None, k) for other in range(k))
            if on_pool(p, k):
                return UNITS + POOL_UNITS * (p - 1) + before + 1
            return (UNITS - POOL_UNITS) * (p - 1) + before + 1

        def loads_of_slot(p, m):
            return PAIRS // BUFS * p + m // BUFS + 1

        def row_tile(k):
            source = even if k % PAIR < Q else odd
            return source[:, k // PAIR % BUFS, k % Q, :]

        def col_tile(k):
            return 2 * (k // PAIR) + k % 2, k % PAIR // 2

        def tile_columns(cols, c):
            return cols.rearrange("p (i c) -> p c i", c=Q)[:, c]

        @block.sync
        def _(sp):
            def load_x(g):
                first, end = X_GROUPS[g]
                sp.dma_start(x_sb[:, Q * first:Q * end, :].rearrange("p (k c) d -> p k (c d)", c=Q),
                             x_chunks[first:end].rearrange("k p e -> p k e")).then_inc(x_loaded[g], 16)

            def load_pairs(p):
                for m in range(PAIRS):
                    slot = m % BUFS
                    before = UNITS * p + PAIR * (m - BUFS)
                    col = 2 * m * BW
                    wait(sp, col_used, before + Q + 1)
                    sp.dma_start(even[:, slot], adj_panels[p][:, :, col:col + BW]).then_inc(even_loaded[slot], 16)
                    if first_panel(p) and m == 0:
                        load_x(1)
                    wait(sp, col_used, before + PAIR - 1)
                    for a in range(Q):
                        quad = col + BW + P * a
                        sp.dma_start(squares[S * a:S * a + S, slot], adj_squares[p][:, :, quad:quad + P]
                                     ).then_inc(squares_loaded[slot], 16)
                    if first_panel(p) and m < 2:
                        load_x(m + 2)
                    wait(sp, col_used, before + PAIR)
                    sp.dma_start(odd[:, slot], adj_panels[p][:, :, col + BW:col + 2 * BW]
                                 ).then_inc(odd_loaded[slot], 16)
                    if first_panel(p) and m in (1, 2):
                        load_x(m + 3)

            load_x(0)
            load_pairs(0)
            with sp.Fori(1, PANELS) as p:
                load_pairs(p)

        @block.gpsimd
        def _(pool):
            nc.gpsimd.memset(ident[:, :], 0.0).then_inc(ident_zeroed, 1)
            pool.wait_ge(ident_zeroed, 1)
            nc.gpsimd.affine_select(out=ident[:, :], in_=ident[:, :], compare_op=ALU.not_equal, fill=1.0, base=0,
                                    pattern=[[-1, P]], channel_multiplier=1).then_inc(ident_ready, 1)

            def split_units(p):
                for k in range(UNITS):
                    if on_pool(p, k):
                        pool.wait_ge(row_hi_done, UNITS * p + k + 1)
                        nc.gpsimd.tensor_tensor(row_lo[:, k % RING, :], row_tile(k),
                                                row_hi[:, k % RING, :].bitcast(F32), ALU.subtract
                                                ).then_inc(row_lo_pool, 1)

            split_units(0)
            with pool.Fori(1, PANELS) as p:
                split_units(p)

        @block.tensor
        def _(pe):
            def transpose(k, t):
                source = even[:, k // PAIR % BUFS, t, :]
                return nc.tensor.transpose(tr[k // 2 % 2][:, P * t:P * t + P], tile_columns(source, col_tile(k)[1]),
                                           ident[:, :])

            def wait_transpose(p, k):
                wait(pe, col_lo_done, UNITS * p + k - 3)
                if k % PAIR == 0:
                    pe.wait_ge(even_loaded[k // PAIR % BUFS], 16 * loads_of_slot(p, k // PAIR))

            def project_panel(p):
                pe.wait_ge(out1_copied, p + 1)
                wait(pe, rows_added, p)
                for q in range(Q):
                    last = nc.tensor.matmul(proj_rows[:, P * q:P * q + P], out1_sb[:, P * q:P * q + P], w_in_sb[:, :],
                                            start=True, stop=True)
                last.then_inc(rows_projected, 1)

            def project_chunk(c):
                pe.wait_ge(acc2_added, BLOCKS * LAST + c + 1)
                wait(pe, cols_added, c - 1)
                for q in range(Q):
                    last = nc.tensor.matmul(proj_cols[c % 2][:, P * q:P * q + P],
                                            tile_columns(acc2[:, BW * c:BW * c + BW], q), w_out_sb[:, :],
                                            start=True, stop=True)
                last.then_inc(cols_projected, 1)

            def multiply_units(p, last=False):
                first = first_panel(p)
                for k in range(UNITS):
                    unit = UNITS * p + k
                    b, q, slot = k // Q, k % Q, k % RING
                    if k == Q and not first:
                        project_panel(p - 1)
                    if q == 0 and last and b >= 2:
                        project_chunk(b - 2)
                    ahead = k + AHEAD
                    transposes = k % 2 == 0 and not (last and ahead >= UNITS)
                    if transposes:
                        wait_transpose(*((p, ahead) if ahead < UNITS else (p + 1, ahead - UNITS)))
                        transpose(ahead % UNITS, 0)
                    if on_pool(p, k):
                        pe.wait_ge(row_lo_pool, row_lo_count(p, k))
                    else:
                        pe.wait_ge(row_lo_dve, row_lo_count(p, k))
                    if b == 0:
                        pe.wait_ge(hp_copied, 2 * (Q * p + q + 1))
                    if q == 0:
                        wait(pe, acc2_added, BLOCKS * p + b - 1)
                    o2 = out2[b % 2][:, :]
                    nc.tensor.matmul(o2, hp_hi[:, q, :], row_hi[:, slot, :], start=q == 0, stop=False)
                    if transposes:
                        transpose(ahead % UNITS, 1)
                    nc.tensor.matmul(o2, hp_hi[:, q, :], row_lo[:, slot, :], start=False, stop=False)
                    if transposes:
                        transpose(ahead % UNITS, 2)
                    nc.tensor.matmul(o2, hp_lo[:, q, :], row_hi[:, slot, :], start=False,
                                     stop=q == Q - 1).then_inc(row_used, 1)
                    if transposes:
                        transpose(ahead % UNITS, 3).then_inc(transposed, 1)
                    pe.wait_ge(col_lo_done, unit + 1)
                    if k == 0:
                        wait(pe, out1_copied, p)
                    c, tile = col_tile(k)
                    t = Q * c + tile
                    if first:
                        pe.wait_ge(h_done, c + 1)
                    o1 = out1[:, :]
                    nc.tensor.matmul(o1, h_hi[:, t, :], col_hi[:, slot, :], start=k == 0, stop=False)
                    nc.tensor.matmul(o1, h_hi[:, t, :], col_lo[:, slot, :], start=False, stop=False)
                    nc.tensor.matmul(o1, h_lo[:, t, :], col_hi[:, slot, :], start=False,
                                     stop=k == UNITS - 1).then_inc(col_used, 1)

            pe.wait_ge(ident_ready, 1)
            pe.wait_ge(w_loaded, 32)
            wait_transpose(0, 0)
            for t in range(Q - 1):
                transpose(0, t)
            transpose(0, Q - 1).then_inc(transposed, 1)
            multiply_units(0)
            with pe.Fori(1, LAST) as p:
                multiply_units(p)
            multiply_units(LAST, last=True)
            project_chunk(BLOCKS - 2)
            project_panel(LAST)
            project_chunk(BLOCKS - 1)

        @block.scalar
        def _(act):
            def flat(tiles):
                return tiles.rearrange("p q d -> p (q d)")

            def load_rows(p):
                wait(act, y_stored, 16 * p)
                act.dma_start(flat(rows[:, :, :]), x_chunks[p]).then_inc(rows_loaded, 16)

            def store_y(p):
                act.wait_ge(rows_added, p + 1)
                act.dma_start(y_dram[p], flat(rows[:, :, :])).then_inc(y_stored, 16)

            def load_y(c):
                wait(act, out_stored[c % 2], 16 * (c // 2))
                act.dma_start(flat(chunk[:, c % 2]), y_dram[c]).then_inc(y_loaded[c % 2], 16)

            def store_out(c):
                act.wait_ge(cols_added, c + 1)
                done = chunk[:, c % 2] if c < BLOCKS - 1 else rows[:, :, :]
                act.dma_start(out_chunks[c], flat(done)).then_inc(out_stored[c % 2], 16)

            def deviation(j):
                tiles = slice(2 * Q * j, 2 * Q * j + 2 * Q)
                act.wait_ge(var_done, j + 1)
                nc.scalar.activation(std[:, tiles], var_eps[:, tiles], ACT.Sqrt).then_inc(std_done, 1)

            def high_half_h(c):
                act.wait_ge(norm_done, c + 1)
                nc.scalar.activation(h_hi[:, Q * c:Q * c + Q, :], chunk[:, c % 2], ACT.Relu).then_inc(h_hi_done, 1)

            def copy_out2(b):
                act.wait_ge(row_used, Q * b + Q)
                act.wait_ge(norm_done, b + 1)
                nc.scalar.activation(acc2[:, BW * b:BW * b + BW], out2[b % 2][:, :], ACT.Copy).then_inc(acc2_added, 1)

            def copy_out1(p):
                act.wait_ge(col_used, UNITS * p + UNITS)
                wait(act, rows_projected, p)
                nc.scalar.activation(out1_sb[:, :], out1[:, :], ACT.Copy).then_inc(out1_copied, 1)

            def split_units(p, last=False):
                first = first_panel(p)
                for k in range(UNITS):
                    unit = UNITS * p + k
                    b, q, slot, m = k // Q, k % Q, k % RING, k // PAIR
                    if q == 0:
                        loaded = (even_loaded, odd_loaded)[b % 2][m % BUFS]
                        act.wait_ge(loaded, 16 * loads_of_slot(p, m))
                    if k == 0:
                        wait(act, rowsum_read, p)
                    wait(act, row_used, unit - RING + 1)
                    nc.scalar.activation(row_hi[:, slot, :], row_tile(k), ACT.Copy,
                                         accum_out=rowsum[:, q, b:b + 1]).then_inc(row_hi_done, 1)
                    if k % 2 == 0:
                        act.wait_ge(transposed, HALF * p + k // 2 + 1)
                        source = tr[k // 2 % 2][:, :]
                    else:
                        act.wait_ge(col_t_done, HALF * p + k // 2 + 1)
                        source = col_t[:, k // 2 % 2, :]
                    wait(act, col_used, unit - RING + 1)
                    c, tile = col_tile(k)
                    nc.scalar.activation(col_hi[:, slot, :], source, ACT.Copy,
                                         accum_out=colsum[:, Q * c + tile, bass.ds(p, 1)]).then_inc(col_hi_done, 1)
                    if first:
                        j, kk = k // PAIR, k % PAIR
                        if kk == 0 and j + 1 < PAIRS:
                            deviation(j + 1)
                        if kk in (5, 6) and j + 1 < PAIRS:
                            high_half_h(2 * j + 2 + kk - 5)
                        if q == 2 and b > 0:
                            copy_out2(b - 1)
                    else:
                        if k == 1:
                            copy_out1(p - 1)
                        if b == 3 and q == 0:
                            store_y(p - 1)
                        if b == 5 and q == 0:
                            load_rows(p)
                    if last:
                        if b == 0 and q == 2:
                            load_y(0)
                            load_y(1)
                        if b >= 3 and q == 1:
                            store_out(b - 3)
                        if b >= 3 and q == 3:
                            load_y(b - 1)

            act.dma_start(w_in_sb[:, :], w_in).then_inc(w_loaded, 16)
            act.dma_start(w_out_sb[:, :], w_out).then_inc(w_loaded, 16)
            deviation(0)
            high_half_h(0)
            high_half_h(1)
            load_rows(0)
            split_units(0)
            with act.Fori(1, LAST) as p:
                split_units(p)
            split_units(LAST, last=True)
            copy_out1(LAST)
            for c in range(BLOCKS - 3, BLOCKS):
                store_out(c)
            act.wait_ge(out_stored[0], 16 * BLOCKS // 2)
            act.wait_ge(out_stored[1], 16 * BLOCKS // 2)
            act.wait_ge(y_stored, 16 * LAST)

        @block.vector
        def _(dve):
            STATS, NORM = 2 * Q + 2 * Q, 5
            def tiles_of(j):
                return slice(2 * Q * j, 2 * Q * j + 2 * Q)

            def row_stats(j, first, end):
                if first == 0:
                    dve.wait_ge(x_loaded[next(g for g, (a, z) in enumerate(X_GROUPS) if a <= 2 * j < z)], 16)
                    wait(dve, stats_step, STATS * j)
                for t in range(first, end):
                    nc.vector.bn_stats(stats[:, t, :], x_sb[:, 2 * Q * j + t, :]).then_inc(stats_step, 1)

            def combine_stats(j, first, end):
                dve.wait_ge(stats_step, STATS * j + 2 * Q)
                for t in range(first, end):
                    nc.vector.bn_aggr(mean_var[:, 2 * Q * j + t, :], stats[:, t, :]).then_inc(stats_step, 1)

            def variance(j):
                dve.wait_ge(stats_step, STATS * j + STATS)
                nc.vector.tensor_scalar(var_eps[:, tiles_of(j)], mean_var[:, tiles_of(j), 1], LN_EPS, None,
                                        ALU.add).then_inc(var_done, 1)

            def inverse(j, step):
                a, b = newton[:, 0, :], newton[:, 1, :]
                if step == 0:
                    dve.wait_ge(std_done, j + 1)
                    op = nc.vector.reciprocal(rstd[:, tiles_of(j)], std[:, tiles_of(j)])
                else:
                    dve.wait_ge(norm_step, NORM * j + step)
                if step == 1:
                    op = nc.vector.tensor_tensor(a, rstd[:, tiles_of(j)], rstd[:, tiles_of(j)], ALU.mult)
                if step == 2:
                    op = nc.vector.tensor_tensor(b, a, var_eps[:, tiles_of(j)], ALU.mult)
                if step == 3:
                    op = nc.vector.tensor_scalar(a, b, -0.5, 1.5, ALU.mult, ALU.add)
                if step == 4:
                    op = nc.vector.tensor_tensor(b, rstd[:, tiles_of(j)], a, ALU.mult)
                op.then_inc(norm_step, 1)

            def normalise(c):
                dve.wait_ge(norm_step, NORM * (c // 2) + NORM)
                wait(dve, h_done, c - 1)
                for q in range(Q):
                    t = Q * c + q
                    last = nc.vector.tensor_scalar(chunk[:, c % 2, q, :], x_sb[:, t, :], mean_var[:, t, 0:1],
                                                   newton[:, 1, t % (2 * Q):t % (2 * Q) + 1], ALU.subtract, ALU.mult)
                last.then_inc(norm_done, 1)

            def low_half_h(c):
                tiles = slice(Q * c, Q * c + Q)
                dve.wait_ge(h_hi_done, c + 1)
                nc.vector.scalar_tensor_tensor(h_lo[:, tiles, :], chunk[:, c % 2], 0.0, h_hi[:, tiles, :].bitcast(F32),
                                               ALU.max, ALU.subtract).then_inc(h_done, 1)

            def first_stage(j, place):
                half = Q // 2
                if place in ("0a", "0b", "4b", "5a"):
                    n = half * ("0a", "0b", "4b", "5a").index(place)
                    row_stats(j, n, n + half)
                if place == "5b":
                    combine_stats(j, 0, Q)
                if place == "6b":
                    combine_stats(j, Q, 2 * Q)
                if place == "7b":
                    variance(j)

            def second_stage(j, place):
                if place in ("1a", "1b", "2a", "2b", "3a"):
                    inverse(j, ("1a", "1b", "2a", "2b", "3a").index(place))
                if place == "3b":
                    normalise(2 * j)
                if place == "4a":
                    normalise(2 * j + 1)
                if place == "6a":
                    low_half_h(2 * j)
                if place == "7a":
                    low_half_h(2 * j + 1)

            def make_h(k, place):
                if k == 0 and place == "a":
                    row_stats(1, 0, 2 * Q)
                    combine_stats(1, 0, 2 * Q)
                    variance(1)
                j, place = k // PAIR, f"{k % PAIR}{place}"
                if j + 1 < PAIRS:
                    second_stage(j + 1, place)
                if j + 2 < PAIRS:
                    first_stage(j + 2, place)

            def add_out2(p, b):
                dve.wait_ge(row_used, UNITS * p + Q * b + Q)
                cols = slice(BW * b, BW * b + BW)
                nc.vector.tensor_tensor(acc2[:, cols], out2[b % 2][:, :], acc2[:, cols],
                                        ALU.add).then_inc(acc2_added, 1)

            def reciprocal_of(deg, largest, safe, rdeg, step):
                if step == 0:
                    return nc.vector.tensor_scalar(largest[:, :], deg[:, :], 0.0, None, ALU.max)
                if step == 1:
                    return nc.vector.scalar_tensor_tensor(safe[:, :], deg[:, :], 0.0, largest[:, :], ALU.is_le, ALU.add)
                return nc.vector.reciprocal(rdeg[:, :], safe[:, :])

            def sum_rows():
                nc.vector.tensor_reduce(row_deg[:, :], rowsum[:, :, :], AX.X, ALU.add).then_inc(rowsum_read, 1)

            def row_degrees(p, step):
                if step == 0:
                    dve.wait_ge(rowsum_read, p + 1)
                else:
                    dve.wait_ge(row_step, 3 * p + step)
                reciprocal_of(row_deg, row_max, row_safe, row_rdeg, step).then_inc(row_step, 1)

            def finish_rows(p):
                dve.wait_ge(rows_loaded, 16 * (p + 1))
                dve.wait_ge(row_step, 3 * p + 3)
                dve.wait_ge(rows_projected, p + 1)
                for q in range(Q):
                    last = nc.vector.scalar_tensor_tensor(rows[:, q, :], proj_rows[:, P * q:P * q + P],
                                                          row_rdeg[:, q:q + 1], rows[:, q, :], ALU.mult, ALU.add)
                last.then_inc(rows_added, 1)

            def column_degrees(j):
                dve.wait_ge(col_hi_done, UNITS * LAST + PAIR * (j + 1))
                nc.vector.tensor_reduce(col_deg[:, :], colsum[:, 2 * Q * j:2 * Q * j + 2 * Q, :], AX.X,
                                        ALU.add).then_inc(col_step, 1)
                for step in range(3):
                    dve.wait_ge(col_step, 4 * j + 1 + step)
                    reciprocal_of(col_deg, col_max, col_safe, col_rdeg, step).then_inc(col_step, 1)

            def finish_chunk(c):
                dve.wait_ge(col_step, 4 * (c // 2) + 4)
                dve.wait_ge(cols_projected, c + 1)
                if c < BLOCKS - 1:
                    dve.wait_ge(y_loaded[c % 2], 16 * (c // 2 + 1))
                else:
                    dve.wait_ge(rows_added, PANELS)
                for q in range(Q):
                    tile = chunk[:, c % 2, q, :] if c < BLOCKS - 1 else rows[:, q, :]
                    t = Q * (c % 2) + q
                    last = nc.vector.scalar_tensor_tensor(tile, proj_cols[c % 2][:, P * q:P * q + P],
                                                          col_rdeg[:, t:t + 1], tile, ALU.mult, ALU.add)
                last.then_inc(cols_added, 1)

            def copy_h(p, q):
                wait(dve, row_used, UNITS * p - Q + q + 1)
                dve.wait_ge(h_done, p + 1)
                nc.vector.tensor_copy(hp_hi[:, q:q + 1, :], h_hi[:, bass.ds(Q * p + q, 1), :]).then_inc(hp_copied, 1)
                nc.vector.tensor_copy(hp_lo[:, q:q + 1, :], h_lo[:, bass.ds(Q * p + q, 1), :]).then_inc(hp_copied, 1)

            def transpose_odd(p, k):
                slot = k // PAIR % BUFS
                if k % PAIR == 1:
                    dve.wait_ge(squares_loaded[slot], 16 * Q * loads_of_slot(p, k // PAIR))
                tile = squares[:, slot].rearrange("p i (s c) -> p c i s", c=Q)[:, col_tile(k)[1]]
                nc.vector.transpose(col_t[:, k // 2 % 2, :].rearrange("p (t m) -> p m t", t=Q),
                                    tile).then_inc(col_t_done, 1)

            def split_units(p, last=False):
                first = first_panel(p)
                for k in range(UNITS):
                    unit = UNITS * p + k
                    b, q, slot = k // Q, k % Q, k % RING
                    if k % 2 == 0:
                        wait(dve, col_hi_done, unit - 2)
                        wait(dve, col_lo_done, unit - 2)
                        transpose_odd(p, k + 1)
                    if b == 0:
                        copy_h(p, q)
                    if not on_pool(p, k):
                        dve.wait_ge(row_hi_done, unit + 1)
                        nc.vector.tensor_tensor(row_lo[:, slot, :], row_tile(k), row_hi[:, slot, :].bitcast(F32),
                                                ALU.subtract).then_inc(row_lo_dve, 1)
                    if first:
                        make_h(k, "a")
                    dve.wait_ge(col_hi_done, unit + 1)
                    source = tr[k // 2 % 2][:, :] if k % 2 == 0 else col_t[:, k // 2 % 2, :]
                    nc.vector.tensor_tensor(col_lo[:, slot, :], source, col_hi[:, slot, :].bitcast(F32),
                                            ALU.subtract).then_inc(col_lo_done, 1)
                    if first:
                        make_h(k, "b")
                    elif q == 1 and b > 0:
                        add_out2(p, b - 1)
                    elif k == 1:
                        add_out2(p - 1, BLOCKS - 1)
                    if not first and 3 <= k <= 5:
                        row_degrees(p - 1, k - 3)
                    if not first and k == 7:
                        finish_rows(p - 1)
                    if last and b >= 2 and q == 2 and b % 2 == 0:
                        column_degrees(b // 2 - 1)
                    if last and b >= 2 and q == 3:
                        finish_chunk(b - 2)
                sum_rows()

            row_stats(0, 0, 2 * Q)
            combine_stats(0, 0, 2 * Q)
            variance(0)
            for step in range(NORM):
                inverse(0, step)
            normalise(0)
            normalise(1)
            low_half_h(0)
            low_half_h(1)
            split_units(0)
            nc.vector.memset(acc2[:, N - BW:], 0.0).then_inc(last_zeroed, 1)
            dve.wait_ge(last_zeroed, 1)
            with dve.Fori(1, LAST) as p:
                split_units(p)
            split_units(LAST, last=True)
            column_degrees(PAIRS - 1)
            for step in range(3):
                row_degrees(LAST, step)
            add_out2(LAST, BLOCKS - 1)
            finish_chunk(BLOCKS - 2)
            finish_rows(LAST)
            finish_chunk(BLOCKS - 1)


def kernel(**inputs):
    import numpy as _np
    import concourse.bacc as _bacc
    from concourse import mybir as _mybir
    from concourse.bass_utils import run_bass_kernel_spmd as _run

    nc = _bacc.Bacc("TRN2", target_bir_lowering=False, num_devices=1)
    arrays, args = {}, []
    for name in ("x", "adj", "L0_gnn_W_in", "L0_gnn_W_out"):
        a = _np.ascontiguousarray(inputs[name])
        arrays[f"in_{name}"] = a
        args.append(nc.dram_tensor(f"in_{name}", a.shape, _mybir.dt.from_np(a.dtype), kind="ExternalInput").ap())
    shape = inputs["x"].shape
    args.append(nc.dram_tensor("out_0", shape, _mybir.dt.float32, kind="ExternalOutput").ap())
    gnn_layer_kernel(nc, *args)
    r = _run(nc, [arrays], core_ids=[0])
    return r.results[0]["out_0"]
```
